# Optimizing a Trainium2 kernel written in Bass

```python
import numpy as np
import jax
import jax.numpy as jnp

def _softmax(x, axis=-1):
    return jax.nn.softmax(x, axis=axis)

def _gelu(x):
    return jax.nn.gelu(x, approximate=True)

def _silu(x):
    return jax.nn.silu(x)

def _sigmoid(x):
    return jax.nn.sigmoid(x)

def _layernorm(x, axis=-1, eps=1e-05):
    m = jnp.mean(x, axis=axis, keepdims=True)
    v = jnp.var(x, axis=axis, keepdims=True)
    return (x - m) / jnp.sqrt(v + eps)

def _scatter_add(tgt, idx, src, axis=0):
    return tgt.at[idx].add(src)

def _segment_sum(src, seg, n):
    return jax.ops.segment_sum(src, seg, n)
kernel_name = 'mk_adj_preln_d2_adj_r2_1636cf'

def setup_inputs(seed: int=0):
    np.random.seed(seed)
    _w = jnp.asarray

    def _rec_inputs():
        import jax
        import jax.numpy as jnp
        _gk = jax.random.key(seed)
        x = -4.645e-05 + 0.05002 * jax.random.normal(jax.random.fold_in(_gk, 1), (4096, 128), jnp.float32)
        _a = jax.random.bernoulli(jax.random.fold_in(_gk, 2), 0.000976562, (4096, 4096))
        _a = jnp.logical_or(_a, jnp.swapaxes(_a, -1, -2))
        _a = jnp.logical_or(_a, jnp.eye(4096, dtype=bool))
        _af = _a.astype(jnp.float32)
        _af = _af / jnp.maximum(_af.sum(-1, keepdims=True), 1.0)
        adj = _af
        return (x, adj)
    x, adj = _rec_inputs()

    def _L0_gnn_setup():
        import jax, jax.numpy as jnp
        import numpy as np
        EPS = 1e-07
        MAX_TANH = 1.0 - 1e-06

        def _norm(v):
            return jnp.maximum(jnp.linalg.norm(v, axis=-1, keepdims=True), EPS)

        def log_map_zero(y):
            n = _norm(y)
            return jnp.arctanh(jnp.clip(n, 0.0, MAX_TANH)) * y / n

        def exp_map_zero(v):
            n = _norm(v)
            return jnp.tanh(n) * v / n

        def h_add(x, y):
            xy = jnp.sum(x * y, axis=-1, keepdims=True)
            x2 = jnp.sum(x * x, axis=-1, keepdims=True)
            y2 = jnp.sum(y * y, axis=-1, keepdims=True)
            num = (1.0 + 2.0 * xy + y2) * x + (1.0 - x2) * y
            den = 1.0 + 2.0 * xy + x2 * y2
            return num / jnp.maximum(den, EPS)

        def h_mul(x, W):
            return exp_map_zero(log_map_zero(x) @ W)
        key = jax.random.key(seed)
        k1, k2, k3, k4 = jax.random.split(key, 4)
        N, F_IN, F_OUT = (4096, 128, 128)
        x = 0.05 * jax.random.normal(k1, (N, F_IN), dtype=jnp.float32)
        a = (jax.random.uniform(k2, (N, N)) < 0.01).astype(jnp.float32)
        adj = a / jnp.maximum(a.sum(axis=1, keepdims=True), 1.0)
        lim_e = np.sqrt(6.0 / (F_IN + F_IN)) * np.sqrt(2.0)
        lim_l = np.sqrt(6.0 / (2 * F_IN + F_OUT)) * np.sqrt(2.0)
        embed = jax.random.uniform(k3, (F_IN, F_IN), minval=-lim_e, maxval=lim_e, dtype=jnp.float32)
        layer = jax.random.uniform(k4, (2 * F_IN, F_OUT), minval=-lim_l, maxval=lim_l, dtype=jnp.float32)
        embed_bias = jnp.zeros((F_IN,), dtype=jnp.float32)
        layer_bias = jnp.zeros((F_OUT,), dtype=jnp.float32)
        return {'x': x, 'adj': adj, 'embed': embed, 'layer': layer, 'embed_bias': embed_bias, 'layer_bias': layer_bias}
    _L0_gnn_all = _L0_gnn_setup()
    _L0_gnn_in = {k: v for k, v in _L0_gnn_all.items() if k in ('embed', 'layer', 'embed_bias', 'layer_bias')}
    del _L0_gnn_all

    def _L1_gnn_setup():
        import jax, jax.numpy as jnp
        import numpy as np
        N = 4096
        F_IN = 128
        F_OUT = 128
        BLOCK = 64

        def _graph_pool(out, adj):
            neg = jnp.asarray(jnp.finfo(out.dtype).min, out.dtype)

            def body(_, adj_blk):
                masked = jnp.where(adj_blk[:, :, None] != 0, out[None, :, :], neg)
                return (None, jnp.max(masked, axis=1))
            _, blocks = jax.lax.scan(body, None, adj.reshape(N // BLOCK, BLOCK, N))
            return blocks.reshape(N, out.shape[-1])
        key = jax.random.key(seed)
        k_in, k_adj, k_w, k_b = jax.random.split(key, 4)
        x = jax.random.normal(k_in, (N, F_IN), dtype=jnp.float32)
        adj = (jax.random.uniform(k_adj, (N, N)) < 0.01).astype(jnp.float32)
        adj = adj.at[jnp.arange(N), jnp.arange(N)].set(1.0)
        stdv = 1.0 / np.sqrt(F_OUT)
        weight = jax.random.uniform(k_w, (F_IN, F_OUT), minval=-stdv, maxval=stdv, dtype=jnp.float32)
        bias = jax.random.uniform(k_b, (F_OUT,), minval=-stdv, maxval=stdv, dtype=jnp.float32)
        return {'input': x, 'adj': adj, 'weight': weight, 'bias': bias}
    _L1_gnn_all = _L1_gnn_setup()
    _L1_gnn_in = {k: v for k, v in _L1_gnn_all.items() if k in ('weight', 'bias')}
    del _L1_gnn_all
    return {'x': x, 'adj': adj, 'L0_gnn_embed': _L0_gnn_in['embed'], 'L0_gnn_layer': _L0_gnn_in['layer'], 'L0_gnn_embed_bias': _L0_gnn_in['embed_bias'], 'L0_gnn_layer_bias': _L0_gnn_in['layer_bias'], 'L1_gnn_weight': _L1_gnn_in['weight'], 'L1_gnn_bias': _L1_gnn_in['bias']}

def reference(x, adj, L0_gnn_embed, L0_gnn_layer, L0_gnn_embed_bias, L0_gnn_layer_bias, L1_gnn_weight, L1_gnn_bias):
    import jax
    import jax.numpy as jnp

    def _L0_gnn_ref(x, adj, embed, layer, embed_bias, layer_bias):
        import jax, jax.numpy as jnp
        import numpy as np
        EPS = 1e-07
        MAX_TANH = 1.0 - 1e-06

        def _norm(v):
            return jnp.maximum(jnp.linalg.norm(v, axis=-1, keepdims=True), EPS)

        def log_map_zero(y):
            n = _norm(y)
            return jnp.arctanh(jnp.clip(n, 0.0, MAX_TANH)) * y / n

        def exp_map_zero(v):
            n = _norm(v)
            return jnp.tanh(n) * v / n

        def h_add(x, y):
            xy = jnp.sum(x * y, axis=-1, keepdims=True)
            x2 = jnp.sum(x * x, axis=-1, keepdims=True)
            y2 = jnp.sum(y * y, axis=-1, keepdims=True)
            num = (1.0 + 2.0 * xy + y2) * x + (1.0 - x2) * y
            den = 1.0 + 2.0 * xy + x2 * y2
            return num / jnp.maximum(den, EPS)

        def h_mul(x, W):
            return exp_map_zero(log_map_zero(x) @ W)
        h = h_mul(x, embed)
        h = h_add(h, embed_bias[None, :])
        neigh = exp_map_zero(adj @ log_map_zero(h))
        out = h_mul(jnp.concatenate((x, neigh), axis=1), layer)
        out = h_add(out, layer_bias[None, :])
        return out

    def _L1_gnn_ref(input, adj, weight, bias):
        import jax, jax.numpy as jnp
        import numpy as np
        N = 4096
        F_IN = 128
        F_OUT = 128
        BLOCK = 64

        def _graph_pool(out, adj):
            neg = jnp.asarray(jnp.finfo(out.dtype).min, out.dtype)

            def body(_, adj_blk):
                masked = jnp.where(adj_blk[:, :, None] != 0, out[None, :, :], neg)
                return (None, jnp.max(masked, axis=1))
            _, blocks = jax.lax.scan(body, None, adj.reshape(N // BLOCK, BLOCK, N))
            return blocks.reshape(N, out.shape[-1])
        h = input @ weight
        out = jnp.maximum(adj @ h + bias, 0.0)
        return _graph_pool(out, adj)
    h = jnp.maximum(_layernorm(x, axis=-1), 0.0)
    x = x + _L0_gnn_ref(h, adj, L0_gnn_embed, L0_gnn_layer, L0_gnn_embed_bias, L0_gnn_layer_bias)
    h = jnp.maximum(_layernorm(x, axis=-1), 0.0)
    x = x + _L1_gnn_ref(h, adj, L1_gnn_weight, L1_gnn_bias)
    return x

_drawn_inputs = setup_inputs


def setup_inputs(seed=0):
    import zlib

    import numpy as np

    out = dict(_drawn_inputs(seed))
    spreads = {'L0_gnn_embed_bias': (0.0, 0.1), 'L0_gnn_layer_bias': (0.0, 0.1)}
    factors = {}
    for name, (base, spread) in spreads.items():
        noise = np.random.default_rng([zlib.crc32(name.encode()), seed]).standard_normal(out[name].shape)
        drawn = base * np.exp(spread * noise) if base else spread * noise
        out[name] = jnp.asarray(drawn.astype(out[name].dtype))
    for name, factor in factors.items():
        out[name] = (out[name] * factor).astype(out[name].dtype)
    return out
```

```python
from contextlib import ExitStack

import concourse.bass as bass
from concourse import mybir

F32 = mybir.dt.float32
BF16 = mybir.dt.bfloat16
U32 = mybir.dt.uint32
I32 = mybir.dt.int32
ALU = mybir.AluOpType
ACT = mybir.ActivationFunctionType
AX_X = mybir.AxisListType.X

P = 128
N = 4096
F = 128
T = N // P
GT = 4
G = T // GT
GC = GT * F
CW = 512
NB = N // CW
CJ = 8
NC = T // CJ
CH = 2
NK = T // CH
TOP = 8
SLOTS = 32
CAND = NK * TOP
DEG = SLOTS + 1
PAIR = 2
RINGP = 4
JF = 1088
MAX_ITER = SLOTS * (T // PAIR) // RINGP

FLT_MAX = 3.4028234663852886e38
EPS = 1e-7
EPS2 = EPS * EPS
MAX_TANH = 1.0 - 1e-6
LN_EPS = 1e-5
SERIES_BELOW = 0.25
TANH_SERIES = [-1382.0 / 155925, 62.0 / 2835, -17.0 / 315, 2.0 / 15, -1.0 / 3, 1.0]
ATANH_SERIES = [1.0 / 13, 1.0 / 11, 1.0 / 9, 1.0 / 7, 1.0 / 5, 1.0 / 3, 1.0]


def build_gnn(nc, x, adj, adj_blocks, embed, layer, embed_bias, layer_bias, weight, bias, out):
    with ExitStack() as ctx:
        def sb(name, shape, dt=F32):
            return ctx.enter_context(nc.sbuf_tensor(name, shape, dt))

        def sem(name):
            return ctx.enter_context(nc.semaphore(name))

        pool_table = nc.dram_tensor("pool_table", [N + 1, F], F32, kind="Internal").ap()
        x_mid = nc.dram_tensor("x_mid", [N, F], F32, kind="Internal").ap()
        sorted_lists = nc.dram_tensor("sorted_lists", [N, SLOTS + 1], U32, kind="Internal").ap()

        X = sb("X", [P, T * F])
        S = sb("S", [P, T * F])
        GH = sb("GH", [P, T * F])
        Q = sb("Q", [P, T * F])
        TT = sb("TT", [P, T * F])
        V = sb("V", [P, T * F])
        ring = sb("ring", [P, NC, CJ, CW])
        cand_blk = sb("cand_blk", [P, GT, NK, TOP])
        cand = sb("cand", [P, T, CAND])
        rT = sb("rT", [P, 2, GC])
        out_t = rT[:, 0, :]
        rows_out = rT[:, 1, :].rearrange("p (t f) -> p t f", t=GT)
        w_cat = sb("w_cat", [P, 2 * F])
        w_bot = sb("w_bot", [P, F])
        w_l1 = sb("w_l1", [P, F])
        eb = sb("eb", [P, F])
        lb = sb("lb", [P, F])
        bias_col = sb("bias_col", [P, 1])
        ident = sb("ident", [P, P])
        iota_p = sb("iota_p", [P, 1], I32)
        iota_pf = sb("iota_pf", [P, CH])
        diag = sb("diag", [P, CH, P], BF16)
        ones = sb("ones", [P, P])
        ones_bf = sb("ones_bf", [P, P], BF16)
        below = sb("below", [P, P], BF16)
        base = sb("base", [P, CAND])
        list_mem = sb("list_mem", [P, JF], U32)
        lists = list_mem[:, 0:T * (SLOTS + 1)].rearrange("p (t s) -> p t s", t=T)
        job_idx = list_mem[:, :]
        slists = cand[:, :, :].rearrange("p t c -> p (t c)")[:, 0:T * (SLOTS + 1)].bitcast(U32).rearrange("p (t s) -> p t s", t=T)
        top = sb("top", [P, SLOTS])
        keys2 = sb("keys2", [P, 2, CAND])
        base_i = keys2[:, 1, :].bitcast(I32)
        deg = sb("deg", [P, T])
        rank = sb("rank", [P, T])
        rank_u = sb("rank_u", [P, T], U32)
        jobs_k = sb("jobs_k", [1, 4 * SLOTS])
        jobs_i = sb("jobs_i", [1, 3 * SLOTS], I32)
        jobs_n = sb("jobs_n", [1, 2], I32)
        job_off = sb("job_off", [1, JF // 2], I32)
        pair_off = sb("pair_off", [1, T // PAIR], I32)
        stage = sb("stage", [P, RINGP * PAIR], U32)
        got = sb("got", [P, RINGP * PAIR * F])
        mask = got[:, :].bitcast(BF16).rearrange("p (u j w) -> p u j w", u=2, j=CH)
        zero_row = sb("zero_row", [1, F])
        neg = sb("neg", [P, NB * NC])
        flags = sb("flags", [P, 4])
        flag_i = sb("flag_i", [1, 1], I32)
        pen = sb("pen", [P, T])
        fall = sb("fall", [P, 4])

        onehot = got[:, :].bitcast(BF16)[:, 0:DEG * T]
        deg_i = TT[:, 2 * DEG * T:3 * DEG * T].bitcast(I32)

        names = ("mu nm vs r2 g2 gb rstd n0sq n0 c0 s0 nv th kap al be nsq n1 c1 z2 zl a1 a2 "
                 "t0 t1 t2 t3 t4 ask mid ans").split()
        R = {n: sb("r_" + n, [P, T]) for n in names}
        b2e = sb("b2e", [P, 1])
        b2l = sb("b2l", [P, 1])

        ps = ctx.enter_context(nc.psum_tensor("ps", [P, 8, 512], F32))

        passed = {e: sem("passed_" + e) for e in ("dve", "pool", "sp")}
        x_in = [sem(f"x_in{i}") for i in range(4)]
        w_in = sem("w_in")
        consts = sem("consts")
        v_step = sem("v_step")
        p_step = sem("p_step")
        asked = sem("asked")
        answered = sem("answered")
        nm_ok = sem("nm_ok")
        cen_ok = sem("cen_ok")
        sq1_ok = sem("sq1_ok")
        relu_ok = sem("relu_ok")
        vs_ok = sem("vs_ok")
        sq2_ok = sem("sq2_ok")
        r2_ok = sem("r2_ok")
        trp_ok = sem("trp_ok")
        rT_ok = sem("rT_ok")
        mmg_ok = sem("mmg_ok")
        g_ok = sem("g_ok")
        q_ok = sem("q_ok")
        gb_ok = sem("gb_ok")
        sq3_ok = sem("sq3_ok")
        ab_ok = sem("ab_ok")
        bb_ok = sem("bb_ok")
        t_ready = sem("t_ready")
        adj_in = [sem(f"adj_in{c}") for c in range(NC)]
        chunk_used = sem("chunk_used")
        neg_ok = sem("neg_ok")
        mask_ready = [sem(f"mask_ready{u}") for u in range(2)]
        keys_made = [sem(f"keys_made{u}") for u in range(2)]
        keys_read = [sem(f"keys_read{u}") for u in range(2)]
        cand_kept = sem("cand_kept")
        acc_made = sem("acc_made")
        acc_read = sem("acc_read")
        nv2_ok = sem("nv2_ok")
        mmq_ok = sem("mmq_ok")
        q2_ok = sem("q2_ok")
        a12_ok = sem("a12_ok")
        qa_ok = sem("qa_ok")
        z_ok = sem("z_ok")
        zz_ok = sem("zz_ok")
        zlb_ok = sem("zlb_ok")
        ab2_ok = sem("ab2_ok")
        lbb_ok = sem("lbb_ok")
        x2_ok = sem("x2_ok")
        x2_out = sem("x2_out")
        nm2_ok = sem("nm2_ok")
        cen2_ok = sem("cen2_ok")
        sq4_ok = sem("sq4_ok")
        relu2_ok = sem("relu2_ok")
        trp2_ok = sem("trp2_ok")
        rT2_ok = sem("rT2_ok")
        mmh_ok = sem("mmh_ok")
        hraw_ok = sem("hraw_ok")
        h_ready = sem("h_ready")
        zrow_out = sem("zrow_out")
        acc1_made = sem("acc1_made")
        outt_ok = sem("outt_ok")
        outt_kept = sem("outt_kept")
        trp3_ok = sem("trp3_ok")
        rows_ok = sem("rows_ok")
        rows_out_sem = sem("rows_out_sem")
        table_done = sem("table_done")
        s2_step = sem("s2_step")
        junk_step = sem("junk_step")
        deg_ok = sem("deg_ok")
        onehot_ok = sem("onehot_ok")
        count_ok = sem("count_ok")
        rank_ok = sem("rank_ok")
        scattered = sem("scattered")
        slists_in = sem("slists_in")
        xs_in = sem("xs_in")
        build_step = sem("build_step")
        jobs_ready = sem("jobs_ready")
        flags_ok = sem("flags_ok")
        flagsum_ok = sem("flagsum_ok")
        flag_ready = sem("flag_ready")
        stage_ok = [sem(f"stage_ok{s}") for s in range(RINGP)]
        got_in = [sem(f"got_in{s}") for s in range(RINGP * PAIR)]
        got_used = sem("got_used")
        y_ok = sem("y_ok")
        y_out = sem("y_out")
        row_in = [sem(f"row_in{u}") for u in range(2)]
        row_used = [sem(f"row_used{u}") for u in range(2)]
        f_step = sem("f_step")
        dense_ok = sem("dense_ok")
        trp4_ok = sem("trp4_ok")
        y4_ok = sem("y4_ok")
        y4_out = sem("y4_out")

        def grp(a, g):
            return a[:, g * GC:(g + 1) * GC]

        def grp3(a, g):
            return grp(a, g).rearrange("p (t f) -> p t f", t=GT)

        def bank3(b):
            return ps[:, b, :].rearrange("p (t f) -> p t f", t=GT)

        def per_row(r, g):
            return R[r][:, g * GT:(g + 1) * GT].unsqueeze(2).to_broadcast([P, GT, F])

        def per_feature(a):
            return a[:, :].unsqueeze(1).to_broadcast([P, GT, F])

        def rows(a, g):
            return R[a][:, g * GT:(g + 1) * GT]

        x_rows = x.rearrange("(t p) f -> p t f", p=P)
        x_mid_rows = x_mid.rearrange("(t p) f -> p t f", p=P)
        out_rows = out.rearrange("(t p) f -> p t f", p=P)

        n_const = 12
        block = ctx.enter_context(nc.Block())

        @block.sync
        def _(sp):
            for i in range(4):
                n = T // 4
                sp.dma_start(X[:, i * n * F:(i + 1) * n * F].rearrange("p (t f) -> p t f", f=F),
                             x_rows[:, i * n:(i + 1) * n, :]).then_inc(x_in[i], 16)
            for dst, src in ((w_cat[:, 0:F], embed), (w_cat[:, F:2 * F], layer[0:F, :]), (w_bot[:, :], layer[F:2 * F, :]),
                             (w_l1[:, :], weight),
                             (eb[:, :], embed_bias.rearrange("(a f) -> a f", a=1).to_broadcast([P, F])),
                             (lb[:, :], layer_bias.rearrange("(a f) -> a f", a=1).to_broadcast([P, F])),
                             (bias_col[:, :], bias.rearrange("(f a) -> f a", a=1))):
                sp.dma_start(dst, src).then_inc(w_in, 16)
            for c in range(NC):
                sp.dma_start(ring[:, c, :, :], adj_blocks[0, :, c * CJ:(c + 1) * CJ, :]).then_inc(adj_in[c], 16)
            with sp.Fori(1, NB) as ib:
                for c in range(NC):
                    sp.wait_ge(chunk_used, NC * ib + (c + 1 - NC))
                    sp.sem_inc(passed["sp"], 1)
                    sp.dma_start(ring[:, c, :, :], adj_blocks[bass.ds(ib, 1), :, c * CJ:(c + 1) * CJ, :]
                                 .rearrange("a p j w -> (a p) j w")).then_inc(adj_in[c], 16)
            for c in range(NC):
                sp.wait_ge(chunk_used, NC * (NB - 1) + c + 1)
                sp.dma_start(ring[:, c, :, :], adj_blocks[0, :, c * CJ:(c + 1) * CJ, :]).then_inc(adj_in[c], 16)
            for g in range(G):
                sp.wait_ge(x2_ok, g + 1)
            sp.dma_start(x_mid_rows, X[:, :].rearrange("p (t f) -> p t f", f=F)).then_inc(x2_out, 16)
            sp.wait_ge(consts, n_const)
            sp.dma_start(pool_table[0:1, :], zero_row[:, :]).then_inc(zrow_out, 16)

            def store_rows(ib):
                sp.wait_ge(rows_ok, ib + 1)
                sp.sem_inc(passed["sp"], 1)
                sp.dma_start(pool_table[bass.ds(ib * CW + 1, CW), :].rearrange("(t p) f -> p t f", p=P),
                             rows_out).then_inc(rows_out_sem, 16)

            with sp.Fori(1, NB) as ib:
                for c in range(NC):
                    sp.wait_ge(chunk_used, NC * ib + (NC * NB + c + 1 - NC))
                    sp.sem_inc(passed["sp"], 1)
                    sp.wait_ge(neg_ok, NC * ib + (c + 1 - NC))
                    sp.sem_inc(passed["sp"], 1)
                    sp.dma_start(ring[:, c, :, :], adj_blocks[bass.ds(ib, 1), :, c * CJ:(c + 1) * CJ, :]
                                 .rearrange("a p j w -> (a p) j w")).then_inc(adj_in[c], 16)
                    if c == NC - 2:
                        store_rows(ib - 1)
            sp.wait_ge(scattered, 16 * T)
            sp.dma_start(slists[:, :, :], sorted_lists.rearrange("(t p) s -> p t s", p=P)).then_inc(slists_in, 16)
            store_rows(NB - 1)
            sp.wait_ge(rows_out_sem, 16 * NB)
            sp.wait_ge(zrow_out, 16)
            sp.wait_ge(x2_out, 16)
            sp.sem_inc(table_done, 1)
            sp.wait_ge(flag_ready, 1)
            flagged = sp.value_load(flag_i[0:1, 0:1], min_val=0, max_val=1)
            with sp.If(flagged > 0):
                for u in range(2):
                    sp.dma_start(ring[:, u, :, :].rearrange("p j w -> p (j w)"),
                                 adj[u:u + 1, :].to_broadcast([P, N])).then_inc(row_in[u], 16)
                with sp.Fori(1, N // 2) as h:
                    for u in range(2):
                        sp.wait_ge(row_used[u], h)
                        sp.sem_inc(passed["sp"], 1)
                        sp.dma_start(ring[:, u, :, :].rearrange("p j w -> p (j w)"),
                                     adj[bass.ds(h * 2 + u, 1), :].to_broadcast([P, N])).then_inc(row_in[u], 16)
                sp.wait_ge(y4_ok, T)
                sp.dma_start(out_rows, S[:, :].rearrange("p (t f) -> p t f", f=F)).then_inc(y4_out, 16)
                sp.wait_ge(y4_out, 16)
            with sp.Else():
                sp.wait_ge(y_out, 16 * T)
            sp.nop()

        @block.gpsimd
        def _(pool):
            g_ = nc.gpsimd
            g_.memset(ident[:, :], 0.0).then_inc(consts, 1)
            pool.wait_ge(consts, 1)
            g_.affine_select(out=ident[:, :], in_=ident[:, :], compare_op=ALU.not_equal, fill=1.0, base=0,
                             pattern=[[-1, P]], channel_multiplier=1).then_inc(consts, 1)
            g_.memset(ones[:, :], 1.0).then_inc(consts, 1)
            g_.memset(ones_bf[:, :], 1.0).then_inc(consts, 1)
            g_.memset(below[:, :], 1.0).then_inc(consts, 1)
            pool.wait_ge(consts, 5)
            g_.affine_select(out=below[:, :], in_=below[:, :], compare_op=ALU.is_gt, fill=0.0, base=0,
                             pattern=[[1, P]], channel_multiplier=-1).then_inc(consts, 1)
            g_.iota(iota_p[:, :], pattern=[[0, 1]], base=1, channel_multiplier=1).then_inc(consts, 1)
            g_.iota(base_i, pattern=[[CH * P, NK], [0, TOP]], base=0, channel_multiplier=0).then_inc(consts, 1)
            g_.iota(lists[:, :, SLOTS:SLOTS + 1], pattern=[[P, T], [0, 1]], base=0, channel_multiplier=1)\
                .then_inc(consts, 1)
            g_.iota(pair_off[:, :], pattern=[[PAIR * F, T // PAIR]], base=0, channel_multiplier=0).then_inc(consts, 1)
            g_.memset(zero_row[:, :], 0.0).then_inc(consts, 1)
            g_.memset(job_off[:, :], 0).then_inc(consts, 1)

            for g in range(G):
                pool.wait_ge(nm_ok, g + 1)
                g_.tensor_tensor(grp3(S, g), grp3(X, g), per_row("nm", g), ALU.add).then_inc(cen_ok, 1)
            for g in range(G):
                pool.wait_ge(g_ok, g + 1)
                pool.wait_ge(vs_ok, g + 1)
                g_.tensor_tensor(grp3(TT, g), grp3(GH, g), per_feature(eb), ALU.mult).then_inc(gb_ok, 1)
            pool.wait_ge(ab_ok, 1)
            for g in range(G):
                g_.tensor_tensor(grp3(S, g), per_feature(eb), per_row("be", g), ALU.mult).then_inc(bb_ok, 1)
            pool.wait_ge(a12_ok, 1)
            for g in range(G):
                g_.tensor_tensor(grp3(S, g), grp3(Q, g), per_row("a1", g), ALU.mult).then_inc(qa_ok, 1)
            for g in range(G):
                pool.wait_ge(z_ok, g + 1)
                g_.tensor_tensor(grp3(V, g), grp3(TT, g), per_feature(lb), ALU.mult).then_inc(zlb_ok, 1)
            pool.wait_ge(ab2_ok, 1)
            for g in range(G):
                g_.tensor_tensor(grp3(V, g), per_feature(lb), per_row("be", g), ALU.mult).then_inc(lbb_ok, 1)
            for g in range(G):
                pool.wait_ge(nm2_ok, g + 1)
                g_.tensor_tensor(grp3(S, g), grp3(X, g), per_row("nm", g), ALU.add).then_inc(cen2_ok, 1)
            pool.wait_ge(h_ready, G)
            g_.iota(deg_i, pattern=[[1, DEG], [0, T]], base=0, channel_multiplier=0).then_inc(deg_ok, 1)
            with pool.Fori(0, NB) as ib:
                pool.wait_ge(outt_ok, ib + 1)
                g_.tensor_copy(V[:, bass.ds(ib * CW, CW)], out_t).then_inc(outt_kept, 1)
            pool.wait_ge(rank_ok, 1)
            for t in range(T):
                g_.indirect_dma_start(out=sorted_lists, out_offset=bass.IndirectOffsetOnAxis(ap=rank_u[:, t:t + 1], axis=0),
                                      in_=lists[:, t, :], in_offset=None).then_inc(scattered, 16)
            pool.wait_ge(slists_in, 16)
            pool.wait_ge(x2_out, 16)
            for t in range(T):
                g_.indirect_dma_start(out=Q[:, t * F:(t + 1) * F], out_offset=None, in_=x_mid,
                                      in_offset=bass.IndirectOffsetOnAxis(ap=slists[:, t, SLOTS:SLOTS + 1], axis=0))\
                    .then_inc(xs_in, 16)
            pool.wait_ge(flag_ready, 1)
            pool.wait_ge(jobs_ready, 1)
            pool.wait_ge(table_done, 1)
            flagged = pool.value_load(flag_i[0:1, 0:1], min_val=0, max_val=1)
            n_iter = pool.value_load(jobs_n[0:1, 0:1], min_val=1, max_val=MAX_ITER)
            with pool.If(flagged < 1):
                with pool.Fori(0, n_iter) as it:
                    for s in range(RINGP):
                        pool.wait_ge(stage_ok[s], it + 1)
                        pool.sem_inc(passed["pool"], 1)
                        for a in range(PAIR):
                            c = s * PAIR + a
                            g_.indirect_dma_start(out=got[:, (s * PAIR + a) * F:(s * PAIR + a + 1) * F], out_offset=None, in_=pool_table,
                                                  in_offset=bass.IndirectOffsetOnAxis(ap=stage[:, c:c + 1], axis=0))\
                                .then_inc(got_in[c], 16)
                for t in range(T):
                    pool.wait_ge(y_ok, t // GT + 1)
                    g_.indirect_dma_start(out=out, out_offset=bass.IndirectOffsetOnAxis(ap=slists[:, t, SLOTS:SLOTS + 1], axis=0),
                                          in_=S[:, t * F:(t + 1) * F], in_offset=None).then_inc(y_out, 16)
                pool.wait_ge(y_out, 16 * T)
            with pool.Else():
                pool.nop()
            pool.nop()

        @block.scalar
        def _(act):
            a_ = nc.scalar
            n_asked = [0]
            n_answered = [0]

            def ask():
                n_asked[0] += 1
                act.wait_ge(asked, n_asked[0])

            def answer(ins):
                n_answered[0] += 1
                ins.then_inc(answered, 1)

            def root():
                ask()
                answer(a_.activation(R["mid"][:, :], R["ask"][:, :], ACT.Ln))
                act.wait_ge(answered, n_answered[0])
                answer(a_.activation(R["ans"][:, :], R["mid"][:, :], ACT.Exp, scale=0.5))

            def exp_m2():
                ask()
                answer(a_.activation(R["ans"][:, :], R["ask"][:, :], ACT.Exp, scale=-2.0))

            def two_logs():
                ask()
                answer(a_.activation(R["mid"][:, :], R["ask"][:, :], ACT.Ln, bias=1.0))
                answer(a_.activation(R["ans"][:, :], R["ask"][:, :], ACT.Ln, bias=1.0, scale=-1.0))

            for g in range(G):
                act.wait_ge(cen_ok, g + 1)
                a_.activation(grp(TT, g), grp(S, g), ACT.Square).then_inc(sq1_ok, 1)
                act.wait_ge(relu_ok, g + 1)
                act.wait_ge(sq1_ok, g + 1)
                a_.activation(grp(S, g), grp(V, g), ACT.Square).then_inc(sq2_ok, 1)
                act.wait_ge(trp_ok, g + 1)
                if g >= 2:
                    act.wait_ge(mmg_ok, g - 1)
                a_.activation(rT[:, g % 2, :], ps[:, g % 2, :], ACT.Copy).then_inc(rT_ok, 1)
                act.wait_ge(mmg_ok, g + 1)
                a_.activation(grp(GH, g), ps[:, 2 + 2 * (g % 2), :], ACT.Copy).then_inc(g_ok, 1)
                act.wait_ge(g_ok, g + 1)
                act.wait_ge(r2_ok, g + 1)
                a_.activation(grp(S, g), grp(GH, g), ACT.Square).then_inc(sq3_ok, 1)
            root()
            root()
            two_logs()
            root()
            exp_m2()
            root()
            two_logs()
            with act.Fori(0, NB) as ib:
                for m in range(NK):
                    if m % (NK // NC) == 0:
                        act.wait_ge(adj_in[m // (NK // NC)], 16 * ib + 16)
                    act.wait_ge(keys_made[m % 2], (NK // 2) * ib + m // 2)
                    j = m % (NK // NC) * CH
                    a_.activation(mask[:, m % 2, :, :], ring[:, m // (NK // NC), j:j + CH, :], ACT.Sign)\
                        .then_inc(mask_ready[m % 2], 1)
                act.wait_ge(acc_made, ib + 1)
                a_.activation(V[:, bass.ds(ib * CW, CW)], ps[:, 0, :], ACT.Copy).then_inc(acc_read, 1)
                a_.activation(S[:, bass.ds(ib * CW, CW)], ps[:, 0, :], ACT.Square).then_inc(acc_read, 1)
            for g in range(G):
                act.wait_ge(mmq_ok, g + 1)
                a_.activation(grp(GH, g), ps[:, 1 + g % 2, :], ACT.Copy).then_inc(q2_ok, 1)
            root()
            exp_m2()
            root()
            two_logs()
            for g in range(G):
                act.wait_ge(z_ok, g + 1)
                a_.activation(grp(S, g), grp(TT, g), ACT.Square).then_inc(zz_ok, 1)
            root()
            exp_m2()
            for g in range(G):
                act.wait_ge(cen2_ok, g + 1)
                a_.activation(grp(TT, g), grp(S, g), ACT.Square).then_inc(sq4_ok, 1)
                act.wait_ge(trp2_ok, g + 1)
                if g >= 2:
                    act.wait_ge(mmh_ok, g - 1)
                a_.activation(rT[:, g % 2, :], ps[:, 3 + g % 2, :], ACT.Copy).then_inc(rT2_ok, 1)
                act.wait_ge(mmh_ok, g + 1)
                a_.activation(grp(GH, g), ps[:, 5 + g % 2, :], ACT.Copy).then_inc(hraw_ok, 1)
            root()

            def rows_of(ib):
                act.wait_ge(trp3_ok, ib + 1)
                act.wait_ge(rows_out_sem, 16 * ib)
                a_.activation(rows_out, bank3(1), ACT.Copy).then_inc(rows_ok, 1)

            def l1_block(ib, first=False):
                for c in range(NC):
                    act.wait_ge(adj_in[c], 16 * ib + 16 * (NB + 1))
                    act.wait_ge(junk_step, NC * ib + c)
                    a_.activation(S[:, :], ring[:, c, :, :].rearrange("p j w -> p (j w)"), ACT.Relu, scale=-1.0,
                                  accum_out=neg[:, bass.ds(ib * NC + c, 1)]).then_inc(neg_ok, 1)
                    act.wait_ge(neg_ok, NC * ib + c + 1)
                    act.sem_inc(junk_step, 1)
                    if c == 1 and not first:
                        rows_of(ib - 1)
                act.wait_ge(acc1_made, ib + 1)
                act.wait_ge(outt_kept, ib)
                act.wait_ge(trp3_ok, ib)
                a_.activation(out_t, ps[:, 0, :], ACT.Relu, bias=bias_col[:, 0:1]).then_inc(outt_ok, 1)

            l1_block(0, True)
            with act.Fori(1, NB) as ib:
                l1_block(ib)
            rows_of(NB - 1)

        @block.tensor
        def _(pe):
            pe.wait_ge(consts, n_const)
            pe.wait_ge(w_in, 16 * 7)
            for g in range(G):
                pe.wait_ge(relu_ok, g + 1)
                if g >= 2:
                    pe.wait_ge(rT_ok, g - 1)
                for t in range(GT):
                    mm = pe.transpose(ps[:, g % 2, t * F:(t + 1) * F], V[:, (g * GT + t) * F:(g * GT + t + 1) * F], ident[:, :])
                mm.then_inc(trp_ok, 1)
                pe.wait_ge(rT_ok, g + 1)
                if g >= 2:
                    pe.wait_ge(g_ok, g - 1)
                    pe.wait_ge(q_ok, g - 1)
                for t in range(GT):
                    for w in range(2):
                        mm = pe.matmul(ps[:, 2 + w + 2 * (g % 2), t * F:(t + 1) * F], rT[:, g % 2, t * F:(t + 1) * F],
                                       w_cat[:, w * F:(w + 1) * F], start=True, stop=True)
                mm.then_inc(mmg_ok, 1)
            pe.wait_ge(q_ok, G)
            with pe.Fori(0, NB) as ib:
                for m in range(NK):
                    if m % (NK // NC) == 0:
                        pe.wait_ge(adj_in[m // (NK // NC)], 16 * ib + 16)
                    pe.wait_ge(mask_ready[m % 2], (NK // 2) * ib + m // 2 + 1)
                    pe.wait_ge(keys_read[m % 2], (NK // 2) * ib + m // 2)
                    for t in range(GT):
                        for j in range(CH):
                            mm = pe.matmul(ps[:, 4 + 2 * (m % 2) + t // 2,
                                              (t % 2) * CH * P + j * P:(t % 2) * CH * P + (j + 1) * P],
                                           mask[:, m % 2, j, t * P:(t + 1) * P], diag[:, j, :], start=True, stop=True)
                    mm.then_inc(keys_made[m % 2], 1)
                    if m == 0:
                        pe.wait_ge(acc_read, 2 * ib)
                    if m % (GT // CH) == 0:
                        pe.wait_ge(t_ready, m // (GT // CH) + 1)
                    for j in range(CH):
                        jb = m * CH + j
                        mm = pe.matmul(ps[:, 0, :], TT[:, jb * F:(jb + 1) * F],
                                       ring[:, jb // CJ, jb % CJ, :], start=(jb == 0), stop=(jb == T - 1))
                    if m == NK - 1:
                        mm.then_inc(acc_made, 1)
                        pe.wait_ge(acc_made, ib + 1)
                        pe.sem_inc(chunk_used, 1)
                    elif m % (NK // NC) == NK // NC - 1:
                        mm.then_inc(chunk_used, 1)
            pe.wait_ge(acc_read, 2 * NB)
            for t in range(T):
                mm = pe.matmul(ps[:, 0, t:t + 1], S[:, t * P:(t + 1) * P], ones[:, 0:1], start=True, stop=True)
            mm.then_inc(nv2_ok, 1)
            for g in range(G):
                if g >= 2:
                    pe.wait_ge(q2_ok, g - 1)
                for t in range(GT):
                    mm = pe.matmul(ps[:, 1 + g % 2, t * F:(t + 1) * F], V[:, (g * GT + t) * P:(g * GT + t + 1) * P],
                                   w_bot[:, :], start=True, stop=True)
                mm.then_inc(mmq_ok, 1)
            for g in range(G):
                pe.wait_ge(relu2_ok, g + 1)
                if g >= 2:
                    pe.wait_ge(rT2_ok, g - 1)
                for t in range(GT):
                    mm = pe.transpose(ps[:, 3 + g % 2, t * F:(t + 1) * F], V[:, (g * GT + t) * F:(g * GT + t + 1) * F], ident[:, :])
                mm.then_inc(trp2_ok, 1)
                pe.wait_ge(rT2_ok, g + 1)
                if g >= 2:
                    pe.wait_ge(hraw_ok, g - 1)
                for t in range(GT):
                    mm = pe.matmul(ps[:, 5 + g % 2, t * F:(t + 1) * F], rT[:, g % 2, t * F:(t + 1) * F], w_l1[:, :],
                                   start=True, stop=True)
                mm.then_inc(mmh_ok, 1)
            pe.wait_ge(hraw_ok, G)

            def turn_rows(ib):
                pe.wait_ge(outt_ok, ib + 1)
                pe.wait_ge(rows_ok, ib)
                for t in range(GT):
                    mm = pe.transpose(ps[:, 1, t * F:(t + 1) * F], out_t[:, t * P:(t + 1) * P], ident[:, :])
                mm.then_inc(trp3_ok, 1)

            def l1_block(ib, first=False):
                pe.wait_ge(outt_ok, ib)
                for jb in range(T):
                    if jb % CJ == 0:
                        pe.wait_ge(adj_in[jb // CJ], 16 * ib + 16 * (NB + 1))
                    if first and jb % GT == 0:
                        pe.wait_ge(h_ready, jb // GT + 1)
                    mm = pe.matmul(ps[:, 0, :], GH[:, jb * F:(jb + 1) * F], ring[:, jb // CJ, jb % CJ, :],
                                   start=(jb == 0), stop=(jb == T - 1))
                    if jb == T - 1:
                        mm.then_inc(acc1_made, 1)
                        pe.wait_ge(acc1_made, ib + 1)
                        pe.sem_inc(chunk_used, 1)
                    elif jb % CJ == CJ - 1:
                        mm.then_inc(chunk_used, 1)
                    if jb == CJ - 1 and not first:
                        turn_rows(ib - 1)

            l1_block(0, True)
            with pe.Fori(1, 5) as ib:
                l1_block(ib)
            pe.wait_ge(onehot_ok, 1)
            for b, lhs in ((2, below), (5, ones_bf)):
                for k, c in enumerate(range(0, DEG * T, 512)):
                    w = min(512, DEG * T - c)
                    mm = pe.matmul(ps[:, b + k, 0:w], lhs[:, :], onehot[:, c:c + w], start=True, stop=True)
            mm.then_inc(count_ok, 1)
            with pe.Fori(5, NB) as ib:
                l1_block(ib)
            turn_rows(NB - 1)
            pe.wait_ge(flags_ok, 1)
            pe.matmul(ps[:, 0, 0:1], ones[:, :], flags[:, 0:1], start=True, stop=True).then_inc(flagsum_ok, 1)
            pe.wait_ge(flag_ready, 1)
            flagged = pe.value_load(flag_i[0:1, 0:1], min_val=0, max_val=1)
            with pe.If(flagged > 0):
                pe.wait_ge(dense_ok, 1)
                for t in range(T):
                    if t >= 2:
                        pe.wait_ge(y4_ok, t - 1)
                    pe.transpose(ps[:, 2 + t % 2, 0:F], TT[:, t * P:(t + 1) * P], ident[:, :]).then_inc(trp4_ok, 1)
            with pe.Else():
                pe.nop()
            pe.nop()

        @block.vector
        def _(dve):
            v_ = nc.vector
            n_step = [0]
            n_asked = [0]
            n_answered = [0]

            def step(ins):
                n_step[0] += 1
                ins.then_inc(v_step, 1)
                dve.wait_ge(v_step, n_step[0])

            def ts(o, a, s1, s2=None, op0=ALU.mult, op1=None):
                step(v_.tensor_scalar(o, a, s1, s2, op0, op1) if op1 is not None else v_.tensor_scalar(o, a, s1, s2, op0))

            def tt(o, a, b, op):
                step(v_.tensor_tensor(o, a, b, op))

            def stt(o, a, s, b, op0, op1):
                step(v_.scalar_tensor_tensor(out=o, in0=a, scalar=s, in1=b, op0=op0, op1=op1))

            def r(n):
                return R[n][:, :]

            def ask_scalar(steps):
                n_asked[0] += 1
                dve.sem_inc(asked, 1)
                n_answered[0] += steps
                dve.wait_ge(answered, n_answered[0])

            def root(o, a, least):
                ts(r("ask"), r(a), least, None, ALU.max)
                ask_scalar(2)
                step(v_.reciprocal(r("t0"), r("ans")))
                tt(r("t0"), r("t0"), r("ask"), ALU.mult)
                tt(r("t0"), r("t0"), r("ans"), ALU.add)
                ts(r(o), r("t0"), 0.5)

            def blend(o, n, n_sq, series, exact):
                ts(r("t1"), r(n_sq), SERIES_BELOW ** 2, None, ALU.min)
                ts(r("t2"), r("t1"), series[0])
                for c in series[1:-1]:
                    stt(r("t2"), r("t2"), c, r("t1"), ALU.add, ALU.mult)
                ts(r("t2"), r("t2"), series[-1], None, ALU.add)
                tt(r("t2"), r("t2"), r(exact), ALU.subtract)
                stt(r("t2"), r(n), SERIES_BELOW, r("t2"), ALU.is_lt, ALU.mult)
                tt(r(o), r("t2"), r(exact), ALU.add)

            def tanh_over(o, n, n_sq):
                ts(r("ask"), r(n), 1.0)
                ask_scalar(1)
                ts(r("t0"), r("ans"), 1.0, None, ALU.add)
                tt(r("t0"), r("t0"), r(n), ALU.mult)
                step(v_.reciprocal(r("t0"), r("t0")))
                ts(r("t3"), r("ans"), -1.0, 1.0, ALU.mult, ALU.add)
                tt(r("t3"), r("t3"), r("t0"), ALU.mult)
                blend(o, n, n_sq, TANH_SERIES, "t3")

            def atanh_over(o, n, n_sq):
                ts(r("ask"), r(n), MAX_TANH, None, ALU.min)
                ask_scalar(2)
                tt(r("t3"), r("mid"), r("ans"), ALU.subtract)
                step(v_.reciprocal(r("t0"), r(n)))
                stt(r("t3"), r("t3"), 0.5, r("t0"), ALU.mult, ALU.mult)
                blend(o, n, n_sq, ATANH_SERIES, "t3")

            def mobius(sq, dot, b2):
                tt(r("t1"), r("kap"), r(dot), ALU.mult)
                ts(r("t1"), r("t1"), 2.0, 1.0, ALU.mult, ALU.add)
                tt(r("t2"), r("kap"), r("kap"), ALU.mult)
                tt(r("t2"), r("t2"), r(sq), ALU.mult)
                stt(r("t3"), r("t2"), b2[:, 0:1], r("t1"), ALU.mult, ALU.add)
                ts(r("t3"), r("t3"), EPS, None, ALU.max)
                step(v_.reciprocal(r("t3"), r("t3")))
                ts(r("t1"), r("t1"), b2[:, 0:1], None, ALU.add)
                tt(r("t1"), r("t1"), r("kap"), ALU.mult)
                tt(r("al"), r("t1"), r("t3"), ALU.mult)
                ts(r("t2"), r("t2"), -1.0, 1.0, ALU.mult, ALU.add)
                tt(r("be"), r("t2"), r("t3"), ALU.mult)

            def group_means(g, ok):
                step(v_.tensor_reduce(rows("mu", g), grp3(X, g), AX_X, ALU.add))
                v_.tensor_scalar(rows("nm", g), rows("mu", g), -1.0 / F, None, ALU.mult).then_inc(ok, 1)

            def inverse_deviation():
                ts(r("t4"), r("vs"), 1.0 / F, LN_EPS, ALU.mult, ALU.add)
                root("t4", "t4", LN_EPS / 2)
                step(v_.reciprocal(r("rstd"), r("t4")))

            dve.wait_ge(consts, n_const)
            step(v_.tensor_copy(base[:, :], base_i))
            step(v_.tensor_copy(iota_pf[:, 0:1], iota_p[:, :]))
            ts(iota_pf[:, 1:2], iota_pf[:, 0:1], float(P), None, ALU.add)
            for j in range(CH):
                ts(diag[:, j, :], ident[:, :], iota_pf[:, j:j + 1], None, ALU.mult)
            for g in range(G):
                if g % 2 == 0:
                    dve.wait_ge(x_in[g // 2], 16)
                group_means(g, nm_ok)
            for g in range(G):
                dve.wait_ge(cen_ok, g + 1)
                v_.tensor_scalar(grp(V, g), grp(S, g), 0.0, None, ALU.max).then_inc(relu_ok, 1)
                dve.wait_ge(sq1_ok, g + 1)
                v_.tensor_reduce(rows("vs", g), grp3(TT, g), AX_X, ALU.add).then_inc(vs_ok, 1)
                dve.wait_ge(sq2_ok, g + 1)
                v_.tensor_reduce(rows("r2", g), grp3(S, g), AX_X, ALU.add).then_inc(r2_ok, 1)
                dve.wait_ge(mmg_ok, g + 1)
                v_.tensor_copy(grp(Q, g), ps[:, 3 + 2 * (g % 2), :]).then_inc(q_ok, 1)
                dve.wait_ge(gb_ok, g + 1)
                v_.tensor_reduce(rows("gb", g), grp3(TT, g), AX_X, ALU.add)
                dve.wait_ge(sq3_ok, g + 1)
                step(v_.tensor_reduce(rows("g2", g), grp3(S, g), AX_X, ALU.add))
            for b, b2 in ((eb, b2e), (lb, b2l)):
                step(v_.tensor_tensor(keys2[:, 0, :], b[:, :], b[:, :], ALU.mult))
                step(v_.tensor_reduce(b2[:, 0:1], keys2[:, 0, :], AX_X, ALU.add))
            inverse_deviation()
            tt(r("n0sq"), r("rstd"), r("rstd"), ALU.mult)
            tt(r("n0sq"), r("n0sq"), r("r2"), ALU.mult)
            root("n0", "n0sq", EPS2)
            atanh_over("c0", "n0", "n0sq")
            tt(r("s0"), r("c0"), r("rstd"), ALU.mult)
            tt(r("nsq"), r("s0"), r("s0"), ALU.mult)
            tt(r("nsq"), r("nsq"), r("g2"), ALU.mult)
            root("nv", "nsq", EPS2)
            tanh_over("th", "nv", "nsq")
            tt(r("kap"), r("th"), r("s0"), ALU.mult)
            mobius("g2", "gb", b2e)
            tt(r("t1"), r("al"), r("g2"), ALU.mult)
            tt(r("t2"), r("be"), r("gb"), ALU.mult)
            stt(r("t1"), r("t2"), 2.0, r("t1"), ALU.mult, ALU.add)
            tt(r("nsq"), r("t1"), r("al"), ALU.mult)
            tt(r("t2"), r("be"), r("be"), ALU.mult)
            stt(r("nsq"), r("t2"), b2e[:, 0:1], r("nsq"), ALU.mult, ALU.add)
            root("n1", "nsq", EPS2)
            atanh_over("c1", "n1", "nsq")
            tt(r("al"), r("al"), r("c1"), ALU.mult)
            step(v_.tensor_tensor(r("be"), r("be"), r("c1"), ALU.mult))
            dve.sem_inc(ab_ok, 1)
            for g in range(G):
                step(v_.tensor_tensor(grp3(TT, g), grp3(GH, g), per_row("al", g), ALU.mult))
                dve.wait_ge(bb_ok, g + 1)
                v_.tensor_tensor(grp(TT, g), grp(TT, g), grp(S, g), ALU.add).then_inc(t_ready, 1)
            with dve.Fori(0, NB) as ib:
                dve.wait_ge(cand_kept, ib)
                for m in range(NK):
                    dve.wait_ge(keys_made[m % 2], (NK // 2) * ib + m // 2 + 1)
                    dve.sem_inc(passed["dve"], 1)
                    for t in range(GT):
                        ins = v_.max(cand_blk[:, t, m, :], ps[:, 4 + 2 * (m % 2) + t // 2,
                                                              (t % 2) * CH * P:(t % 2 + 1) * CH * P])
                    ins.then_inc(keys_read[m % 2], 1)
                for u in range(2):
                    dve.wait_ge(keys_read[u], (NK // 2) * ib + NK // 2)
                v_.tensor_copy(cand[:, bass.ds(ib * GT, GT), :], cand_blk[:, :, :, :].rearrange("p t m k -> p t (m k)"))\
                    .then_inc(cand_kept, 1)
            dve.wait_ge(nv2_ok, 1)
            step(v_.tensor_copy(r("nsq"), ps[:, 0, 0:T]))
            root("nv", "nsq", EPS2)
            tanh_over("th", "nv", "nsq")
            tt(r("t4"), r("th"), r("th"), ALU.mult)
            tt(r("t4"), r("t4"), r("nsq"), ALU.mult)
            tt(r("nsq"), r("t4"), r("n0sq"), ALU.add)
            root("n1", "nsq", EPS2)
            atanh_over("c1", "n1", "nsq")
            tt(r("a1"), r("c1"), r("rstd"), ALU.mult)
            tt(r("a2"), r("c1"), r("th"), ALU.mult)
            dve.sem_inc(a12_ok, 1)
            for g in range(G):
                dve.wait_ge(q2_ok, g + 1)
                step(v_.tensor_tensor(grp3(TT, g), grp3(GH, g), per_row("a2", g), ALU.mult))
                dve.wait_ge(qa_ok, g + 1)
                v_.tensor_tensor(grp(TT, g), grp(TT, g), grp(S, g), ALU.add).then_inc(z_ok, 1)
            for g in range(G):
                dve.wait_ge(zz_ok, g + 1)
                v_.tensor_reduce(rows("z2", g), grp3(S, g), AX_X, ALU.add)
                dve.wait_ge(zlb_ok, g + 1)
                step(v_.tensor_reduce(rows("zl", g), grp3(V, g), AX_X, ALU.add))
            root("n1", "z2", EPS2)
            tanh_over("kap", "n1", "z2")
            mobius("z2", "zl", b2l)
            dve.sem_inc(ab2_ok, 1)
            for g in range(G):
                step(v_.tensor_tensor(grp3(TT, g), grp3(TT, g), per_row("al", g), ALU.mult))
                dve.wait_ge(lbb_ok, g + 1)
                step(v_.tensor_tensor(grp(TT, g), grp(TT, g), grp(V, g), ALU.add))
                step(v_.tensor_tensor(grp(X, g), grp(X, g), grp(TT, g), ALU.add))
                dve.sem_inc(x2_ok, 1)
                group_means(g, nm2_ok)
            for g in range(G):
                dve.wait_ge(cen2_ok, g + 1)
                v_.tensor_scalar(grp(V, g), grp(S, g), 0.0, None, ALU.max).then_inc(relu2_ok, 1)
                dve.wait_ge(sq4_ok, g + 1)
                step(v_.tensor_reduce(rows("vs", g), grp3(TT, g), AX_X, ALU.add))
            inverse_deviation()
            for g in range(G):
                dve.wait_ge(hraw_ok, g + 1)
                v_.tensor_tensor(grp3(GH, g), grp3(GH, g), per_row("rstd", g), ALU.mult).then_inc(h_ready, 1)
            steps = 10
            with dve.Fori(0, T) as t:
                k = [0]

                def s2(ins):
                    k[0] += 1
                    ins.then_inc(s2_step, 1)
                    dve.wait_ge(s2_step, steps * t + k[0])
                    dve.sem_inc(passed["dve"], 1)

                row = cand[:, bass.ds(t, 1), :].rearrange("p a c -> p (a c)")
                s2(v_.scalar_tensor_tensor(out=keys2[:, 0, :], in0=row, scalar=0.0, in1=base[:, :],
                                           op0=ALU.is_gt, op1=ALU.mult))
                s2(v_.tensor_tensor(keys2[:, 0, :], keys2[:, 0, :], row, ALU.add))
                for q in range(SLOTS // TOP):
                    s2(v_.max(top[:, q * TOP:(q + 1) * TOP], keys2[:, q % 2, :]))
                    if q < SLOTS // TOP - 1:
                        s2(v_.match_replace(keys2[:, (q + 1) % 2, :], top[:, q * TOP:(q + 1) * TOP], keys2[:, q % 2, :], 0.0))
                s2(v_.tensor_copy(lists[:, bass.ds(t, 1), 0:SLOTS].rearrange("p a s -> p (a s)"), top[:, :]))

                assert k[0] == steps
            full = cand[:, :, :].rearrange("p t (m k) -> p t m k", k=TOP)[:, :, :, TOP - 1]
            step(v_.tensor_reduce(flags[:, 1:2], full, mybir.AxisListType.XY, ALU.max))
            s1 = TT[:, 0:T * SLOTS]
            s13 = s1.rearrange("p (t s) -> p t s", t=T)
            dve.wait_ge(deg_ok, 1)
            ts(s13, lists[:, :, 0:SLOTS], 0.0, None, ALU.is_gt)
            step(v_.tensor_reduce(deg[:, :], s13, AX_X, ALU.add))
            W = DEG * T
            step(v_.tensor_copy(TT[:, 0:W], deg_i))
            step(v_.tensor_tensor(onehot.rearrange("p (d t) -> p d t", t=T),
                                  TT[:, 0:W].rearrange("p (d t) -> p d t", t=T),
                                  deg[:, :].unsqueeze(1).to_broadcast([P, DEG, T]), ALU.is_equal))
            dve.sem_inc(onehot_ok, 1)
            dve.wait_ge(count_ok, 1)
            pre, tot, inc = TT[:, 0:W], TT[:, W:2 * W], TT[:, 2 * W:3 * W]
            for b, dst in ((2, pre), (5, tot)):
                for q, c in enumerate(range(0, W, 512)):
                    w = min(512, W - c)
                    step(v_.tensor_copy(dst[:, c:c + w], ps[:, b + q, 0:w]))
            step(v_.tensor_tensor_scan(inc, tot, tot, 0.0, ALU.add, ALU.bypass))
            tt(pre, pre, inc, ALU.add)
            tt(pre, pre, tot, ALU.subtract)
            tt(pre, pre, onehot, ALU.mult)
            step(v_.tensor_reduce(rank[:, :], pre.rearrange("p (d t) -> p t d", t=T), AX_X, ALU.add))
            ts(rank_u[:, :], rank[:, :], -1.0, float(N - 1), ALU.mult, ALU.add)
            dve.sem_inc(rank_ok, 1)
            jk, ji = jobs_k, jobs_i
            last_of = inc[0:1, :].rearrange("p (d t) -> p d t", t=T)[:, 0:SLOTS, T - 1]
            ts(ji[:, 0:SLOTS], last_of, -1.0, float(N + PAIR * P - 1), ALU.mult, ALU.add)
            ts(ji[:, SLOTS:2 * SLOTS], ji[:, 0:SLOTS], 8, None, ALU.arith_shift_right)
            step(v_.tensor_copy(jk[:, 0:SLOTS], ji[:, SLOTS:2 * SLOTS]))
            step(v_.tensor_tensor_scan(jk[:, SLOTS:2 * SLOTS], jk[:, 0:SLOTS], jk[:, 0:SLOTS], 0.0, ALU.add, ALU.bypass))
            tt(ji[:, 2 * SLOTS:3 * SLOTS], jk[:, SLOTS:2 * SLOTS], jk[:, 0:SLOTS], ALU.subtract)
            ts(jobs_n[:, 1:2], jk[:, 2 * SLOTS - 1:2 * SLOTS], float(RINGP - 1), None, ALU.add)
            ts(jobs_n[:, 0:1], jobs_n[:, 1:2], 2, None, ALU.arith_shift_right)
            ts(jobs_n[:, 0:1], jobs_n[:, 0:1], 1.0, None, ALU.max)
            dve.wait_ge(slists_in, 16)
            step(v_.memset(job_idx, 0))
            by_slot = slists[:, :, :].rearrange("p t s -> p s t")
            with dve.Fori(0, SLOTS) as k:
                off = dve.value_load(ji[0:1, bass.ds(k + 2 * SLOTS, 1)], min_val=0, max_val=(SLOTS - 1) * T // PAIR)
                dve.wait_ge(build_step, 2 * k)
                v_.tensor_copy(job_idx[:, bass.ds(off * PAIR, T)], by_slot[:, bass.ds(k, 1), :].rearrange("p a t -> p (a t)"))\
                    .then_inc(build_step, 1)
                v_.tensor_copy(job_off[:, bass.ds(off, T // PAIR)], pair_off[:, :]).then_inc(build_step, 1)
            dve.wait_ge(build_step, 2 * SLOTS)
            step(v_.memset(TT[:, :], 0.0))
            step(v_.tensor_copy(stage[:, :], job_idx[:, 0:RINGP * PAIR]))
            dve.sem_inc(jobs_ready, 1)
            ts(pen[:, :], slists[:, :, 0], 0.0, -1.0, ALU.is_gt, ALU.add)
            ts(pen[:, :], pen[:, :], FLT_MAX)
            step(v_.tensor_reduce(flags[:, 2:3], deg[:, :], AX_X, ALU.max))
            ts(flags[:, 2:3], flags[:, 2:3], SLOTS - 0.5, None, ALU.is_gt)
            dve.wait_ge(neg_ok, NB * NC)
            step(v_.tensor_reduce(flags[:, 3:4], neg[:, :], AX_X, ALU.max))
            step(v_.tensor_reduce(flags[:, 0:1], flags[:, 1:4], AX_X, ALU.max))
            ts(flags[:, 0:1], flags[:, 0:1], 0.0, None, ALU.is_gt)
            dve.wait_ge(outt_ok, NB)
            dve.sem_inc(flags_ok, 1)
            dve.wait_ge(flagsum_ok, 1)
            ts(flag_i[:, :], ps[0:1, 0, 0:1], 0.0, None, ALU.is_gt)
            dve.sem_inc(flag_ready, 1)
            flagged = dve.value_load(flag_i[0:1, 0:1], min_val=0, max_val=1)
            n_iter = dve.value_load(jobs_n[0:1, 0:1], min_val=1, max_val=MAX_ITER)
            with dve.If(flagged < 1):
                for s in range(RINGP):
                    dve.sem_inc(stage_ok[s], 1)
                with dve.Fori(0, n_iter) as it:
                    for s in range(RINGP):
                        off = dve.value_load(job_off[0:1, bass.ds(it * RINGP + s, 1)], min_val=0, max_val=(T - PAIR) * F)
                        for a in range(PAIR):
                            dve.wait_ge(got_in[s * PAIR + a], 16 * it + 16)
                        dve.wait_ge(got_used, RINGP * it + s)
                        acc = TT[:, bass.ds(off, PAIR * F)]
                        v_.tensor_tensor(acc, acc, got[:, s * PAIR * F:(s + 1) * PAIR * F], ALU.max).then_inc(got_used, 1)
                        dve.wait_ge(got_used, RINGP * it + s + 1)
                        v_.tensor_copy(stage[:, s * PAIR:(s + 1) * PAIR],
                                       job_idx[:, bass.ds((it * RINGP + (RINGP + s)) * PAIR, PAIR)]).then_inc(stage_ok[s], 1)
                dve.wait_ge(got_used, n_iter * RINGP)
                dve.wait_ge(xs_in, 16 * T)
                for g in range(G):
                    v_.tensor_tensor(grp(S, g), grp(TT, g), grp(Q, g), ALU.add).then_inc(f_step, 1)
                    dve.wait_ge(f_step, g + 1)
                    v_.tensor_tensor(grp3(S, g), grp3(S, g), pen[:, g * GT:(g + 1) * GT].unsqueeze(2).to_broadcast([P, GT, F]),
                                     ALU.add).then_inc(y_ok, 1)
            with dve.Else():
                dve.wait_ge(outt_kept, NB)
                with dve.Fori(0, N // 2) as h:
                    for u in range(2):
                        a_row = ring[:, u, :, :].rearrange("p j w -> p (j w)")
                        dve.wait_ge(row_in[u], 16 * h + 16)
                        v_.tensor_scalar(a_row, a_row, 0.0, None, ALU.not_equal, ALU.max, accum_out=fall[:, 0:1])\
                            .then_inc(f_step, 1)
                        dve.wait_ge(f_step, 8 * h + (4 * u + 1))
                        dve.sem_inc(passed["dve"], 1)
                        v_.tensor_tensor_reduce(out=a_row, in0=a_row, in1=V[:, :], scale=1.0, scalar=0.0,
                                                op0=ALU.mult, op1=ALU.max, accum_out=fall[:, 1:2]).then_inc(f_step, 1)
                        dve.wait_ge(f_step, 8 * h + (4 * u + 2))
                        dve.sem_inc(row_used[u], 1)
                        v_.tensor_scalar(fall[:, 2:3], fall[:, 0:1], -1.0, FLT_MAX, ALU.add, ALU.mult).then_inc(f_step, 1)
                        dve.wait_ge(f_step, 8 * h + (4 * u + 3))
                        v_.tensor_tensor(TT[:, bass.ds(h * 2 + u, 1)], fall[:, 1:2], fall[:, 2:3], ALU.add)\
                            .then_inc(f_step, 1)
                        dve.wait_ge(f_step, 8 * h + (4 * u + 4))
                dve.sem_inc(dense_ok, 1)
                for t in range(T):
                    dve.wait_ge(trp4_ok, t + 1)
                    v_.tensor_tensor(S[:, t * F:(t + 1) * F], ps[:, 2 + t % 2, 0:F], X[:, t * F:(t + 1) * F], ALU.add)\
                        .then_inc(y4_ok, 1)
            dve.nop()


_INS = ["x", "adj", "adj_blocks", "L0_gnn_embed", "L0_gnn_layer", "L0_gnn_embed_bias", "L0_gnn_layer_bias",
        "L1_gnn_weight", "L1_gnn_bias"]


def kernel(**inputs):
    import numpy as _np
    import concourse.bacc as _bacc
    from concourse import mybir as _mybir
    from concourse.bass_utils import run_bass_kernel_spmd as _run

    n = 4096
    adj = _np.asarray(inputs["adj"])
    blocks = adj.reshape(n // 512, 512, n // 128, 128).transpose(0, 3, 2, 1)
    given = dict(inputs, adj_blocks=blocks)
    nc = _bacc.Bacc("TRN2", target_bir_lowering=False, num_devices=1)
    arrays, args = {}, []
    for name in _INS:
        a = _np.ascontiguousarray(given[name])
        arrays[f"in_{name}_dram"] = a
        args.append(nc.dram_tensor(f"in_{name}_dram", a.shape, _mybir.dt.from_np(a.dtype), kind="ExternalInput").ap())
    args.append(nc.dram_tensor("out_dram", (n, 128), _mybir.dt.float32, kind="ExternalOutput").ap())
    build_gnn(nc, *args)
    r = _run(nc, [arrays], core_ids=[0])
    return r.results[0]["out_dram"]
```
